# Optimizing a Trainium2 kernel written in Bass

```python
import numpy as np
import jax
import jax.numpy as jnp

def _softmax(x, axis=-1):
    return jax.nn.softmax(x, axis=axis)

def _gelu(x):
    return jax.nn.gelu(x, approximate=True)

def _silu(x):
    return jax.nn.silu(x)

def _sigmoid(x):
    return jax.nn.sigmoid(x)

def _layernorm(x, axis=-1, eps=1e-05):
    m = jnp.mean(x, axis=axis, keepdims=True)
    v = jnp.var(x, axis=axis, keepdims=True)
    return (x - m) / jnp.sqrt(v + eps)

def _scatter_add(tgt, idx, src, axis=0):
    return tgt.at[idx].add(src)

def _segment_sum(src, seg, n):
    return jax.ops.segment_sum(src, seg, n)
kernel_name = 'mk_cond_resid_d1_seqx_r2_acd5c4'

def setup_inputs(seed: int=0):
    np.random.seed(seed)
    _w = jnp.asarray

    def _rec_inputs():
        import jax
        import jax.numpy as jnp
        _rk = jax.random.key(seed)
        x = -0.000125 + 0.9999 * jax.random.normal(jax.random.fold_in(_rk, 1), (128, 128, 512), jnp.float32)
        _lenS = 128 - jax.random.randint(jax.random.fold_in(_rk, 7), (128,), 0, max(1, 128 // 4) + 1, jnp.int32)
        _lenS2 = 128 - jax.random.randint(jax.random.fold_in(_rk, 8), (128,), 0, max(1, 128 // 4) + 1, jnp.int32)
        cond_1024 = 0.00782532 + 1.00527 * jax.random.normal(jax.random.fold_in(_rk, 11), (128, 512), jnp.float32)
        return (x, cond_1024)
    x, cond_1024 = _rec_inputs()

    def _L0_cond_setup():
        import jax, jax.numpy as jnp
        import numpy as np
        INV_SQRT2 = 0.7071067811865476
        key = jax.random.key(seed)
        k1, k2, k3, k4 = jax.random.split(key, 4)
        B, N, d = (8, 2048, 512)
        scale = 1.0 / np.sqrt(d)
        return {'v': jax.random.normal(k1, (B, N, d), dtype=jnp.float32), 'q_pool': jax.random.normal(k2, (B, d), dtype=jnp.float32), 'W1': jax.random.normal(k3, (d, d), dtype=jnp.float32) * scale, 'b1': jnp.zeros((d,), dtype=jnp.float32), 'W2': jax.random.normal(k4, (d, d), dtype=jnp.float32) * scale, 'b2': jnp.zeros((d,), dtype=jnp.float32)}
    _L0_cond_all = _L0_cond_setup()
    _L0_cond_in = {k: v for k, v in _L0_cond_all.items() if k in ('W1', 'b1', 'W2', 'b2')}
    del _L0_cond_all
    return {'x': x, 'cond_1024': cond_1024, 'L0_cond_W1': _L0_cond_in['W1'], 'L0_cond_b1': _L0_cond_in['b1'], 'L0_cond_W2': _L0_cond_in['W2'], 'L0_cond_b2': _L0_cond_in['b2']}

def reference(x, cond_1024, L0_cond_W1, L0_cond_b1, L0_cond_W2, L0_cond_b2):
    import jax
    import jax.numpy as jnp

    def _L0_cond_ref(v, q_pool, W1, b1, W2, b2):
        import jax, jax.numpy as jnp
        import numpy as np
        INV_SQRT2 = 0.7071067811865476
        B, N, d = v.shape
        h = jax.nn.silu(q_pool @ W1.T + b1)
        gate = jax.nn.sigmoid(h @ W2.T + b2)[:, None, :]
        levels = int(np.log2(N))
        a = v
        details = []
        for _ in range(levels):
            e, o = (a[:, 0::2], a[:, 1::2])
            details.append((e - o) * INV_SQRT2)
            a = (e + o) * INV_SQRT2
        a = a * gate
        for dc in reversed(details):
            dc = dc * gate
            e = (a + dc) * INV_SQRT2
            o = (a - dc) * INV_SQRT2
            n = e.shape[1]
            a = jnp.stack([e, o], axis=2).reshape(B, 2 * n, d)
        return v + a
    x = x + _L0_cond_ref(x, cond_1024, L0_cond_W1, L0_cond_b1, L0_cond_W2, L0_cond_b2)
    return x

_drawn_inputs = setup_inputs


def setup_inputs(seed=0):
    import zlib

    import numpy as np

    out = dict(_drawn_inputs(seed))
    spreads = {'L0_cond_b1': (0.0, 0.8), 'L0_cond_b2': (0.0, 0.8)}
    factors = {}
    for name, (base, spread) in spreads.items():
        noise = np.random.default_rng([zlib.crc32(name.encode()), seed]).standard_normal(out[name].shape)
        drawn = base * np.exp(spread * noise) if base else spread * noise
        out[name] = jnp.asarray(drawn.astype(out[name].dtype))
    for name, factor in factors.items():
        out[name] = (out[name] * factor).astype(out[name].dtype)
    return out
```

```python
from contextlib import ExitStack

import concourse.bass as bass
from concourse import mybir

F32 = mybir.dt.float32
ALU = mybir.AluOpType
ACT = mybir.ActivationFunctionType

P = 128
CHUNK_STEPS = 8
SLOTS = 8
DMA_DONE = 16


def gated_residual_program(nc, x, cond, w1, b1, w2, b2, out):
    B, N, D = x.shape
    BLOCKS = D // P
    CHUNKS = N // CHUNK_STEPS
    ROUNDS = CHUNKS // SLOTS
    assert B == P and D == BLOCKS * P and N == ROUNDS * SLOTS * CHUNK_STEPS and ROUNDS >= 2

    with ExitStack() as ctx:
        def sbuf(name, shape):
            return ctx.enter_context(nc.sbuf_tensor(name, shape, F32))

        def psum(name, shape):
            return ctx.enter_context(nc.psum_tensor(name, shape, F32))

        def sem(name):
            return ctx.enter_context(nc.semaphore(name))

        ring = sbuf("ring", [P, SLOTS, CHUNK_STEPS, D])
        cond_rows = sbuf("cond_rows", [P, D])
        w1_rows = sbuf("w1_rows", [P, BLOCKS, D])
        w2_rows = sbuf("w2_rows", [P, BLOCKS, D])
        b1_cols = sbuf("b1_cols", [P, BLOCKS])
        b2_row = sbuf("b2_row", [1, D])
        identity = sbuf("identity", [P, P])
        ones_row = sbuf("ones_row", [1, P])
        cond_t = sbuf("cond_t", [P, BLOCKS, B])
        w1_t = sbuf("w1_t", [P, BLOCKS, BLOCKS, P])
        w2_t = sbuf("w2_t", [P, BLOCKS, D])
        hidden_sigmoid = sbuf("hidden_sigmoid", [P, BLOCKS, B])
        hidden = sbuf("hidden", [P, BLOCKS, B])
        gate = sbuf("gate", [P, D])
        factor = sbuf("factor", [P, D])

        turned = [psum(f"turned{c}", [P, D]) for c in range(BLOCKS)]
        turned_cond = psum("turned_cond", [P, D])
        hidden_sum = psum("hidden_sum", [P, BLOCKS, B])
        gate_sum = psum("gate_sum", [P, D])

        cond_loaded, w1_loaded, w2_loaded = sem("cond_loaded"), sem("w1_loaded"), sem("w2_loaded")
        b1_loaded, b2_loaded = sem("b1_loaded"), sem("b2_loaded")
        zeros_set, identity_set, ones_set = sem("zeros_set"), sem("identity_set"), sem("ones_set")
        cond_turned, w1_turned, w2_turned = sem("cond_turned"), sem("w1_turned"), sem("w2_turned")
        cond_t_set, w1_t_set, w2_t_set = sem("cond_t_set"), sem("w1_t_set"), sem("w2_t_set")
        hidden_summed, sigmoid_set, hidden_set = sem("hidden_summed"), sem("sigmoid_set"), sem("hidden_set")
        gate_summed, gate_set, factor_set = sem("gate_summed"), sem("gate_set"), sem("factor_set")
        chunk_loaded = [sem(f"chunk_loaded{s}") for s in range(SLOTS)]
        chunk_scaled = sem("chunk_scaled")
        chunk_stored = [sem(f"chunk_stored{s}") for s in range(SLOTS)]

        block = ctx.enter_context(nc.Block())

        def steps(rnd, s):
            return bass.ds(rnd * (SLOTS * CHUNK_STEPS) + s * CHUNK_STEPS, CHUNK_STEPS)

        @block.sync
        def _(sp):
            sp.dma_start(cond_rows[:, :], cond).then_inc(cond_loaded, DMA_DONE)
            sp.dma_start(w1_rows[:, :, :], w1.rearrange("(p t) k -> p t k", t=BLOCKS)).then_inc(w1_loaded, DMA_DONE)
            sp.dma_start(w2_rows[:, :, :], w2.rearrange("(t p) k -> p t k", p=P)).then_inc(w2_loaded, DMA_DONE)
            for s in range(SLOTS):
                sp.dma_start(ring[:, s, :, :], x[:, steps(0, s), :]).then_inc(chunk_loaded[s], DMA_DONE)
            with sp.Fori(1, ROUNDS) as rnd:
                for s in range(SLOTS):
                    sp.wait_ge(chunk_stored[s], rnd * DMA_DONE)
                    sp.dma_start(ring[:, s, :, :], x[:, steps(rnd, s), :]).then_inc(chunk_loaded[s], DMA_DONE)

        @block.gpsimd
        def _(pool):
            pool.memset(identity[:, :], 0.0).then_inc(zeros_set, 1)
            pool.memset(ones_row[:, :], 1.0).then_inc(ones_set, 1)
            pool.wait_ge(zeros_set, 1)
            pool.affine_select(out=identity[:, :], in_=identity[:, :], compare_op=ALU.not_equal, fill=1.0,
                               base=0, pattern=[[-1, P]], channel_multiplier=1).then_inc(identity_set, 1)

        @block.tensor
        def _(pe):
            pe.wait_ge(identity_set, 1)
            pe.wait_ge(cond_loaded, DMA_DONE)
            for c in range(BLOCKS):
                last = pe.transpose(turned_cond[:, c * B:(c + 1) * B], cond_rows[:, c * P:(c + 1) * P], identity[:, :])
            last.then_inc(cond_turned, 1)
            pe.wait_ge(w1_loaded, DMA_DONE)
            for c in range(BLOCKS):
                for t in range(BLOCKS):
                    last = pe.transpose(turned[c][:, t * P:(t + 1) * P], w1_rows[:, t, c * P:(c + 1) * P],
                                        identity[:, :])
                last.then_inc(w1_turned, 1)
            pe.wait_ge(cond_t_set, 1)
            pe.wait_ge(w1_t_set, BLOCKS)
            for t in range(BLOCKS):
                for c in range(BLOCKS):
                    last = pe.matmul(hidden_sum[:, t, :], w1_t[:, c, t, :], cond_t[:, c, :],
                                     start=(c == 0), stop=(c == BLOCKS - 1))
            last.then_inc(hidden_summed, 1)
            pe.wait_ge(w2_loaded, DMA_DONE)
            w2_strided = w2_rows[:, :, :].rearrange("j m (p t) -> j m t p", t=BLOCKS)
            for t in range(BLOCKS):
                for m in range(BLOCKS):
                    last = pe.transpose(turned[t][:, m * P:(m + 1) * P], w2_strided[:, m, t, :], identity[:, :])
                last.then_inc(w2_turned, 1)
            pe.wait_ge(ones_set, 1)
            pe.wait_ge(b2_loaded, DMA_DONE)
            pe.matmul(gate_sum[:, :], ones_row[:, :], b2_row[:, :], start=True, stop=False)
            for t in range(BLOCKS):
                pe.wait_ge(hidden_set, t + 1)
                pe.wait_ge(w2_t_set, t + 1)
                last = pe.matmul(gate_sum[:, :], hidden[:, t, :], w2_t[:, t, :], start=False, stop=(t == BLOCKS - 1))
            last.then_inc(gate_summed, 1)

        @block.scalar
        def _(act):
            act.dma_start(b1_cols[:, :], b1.rearrange("(p t) -> p t", t=BLOCKS)).then_inc(b1_loaded, DMA_DONE)
            act.dma_start(b2_row[:, :], b2.rearrange("(a j) -> a j", a=1)).then_inc(b2_loaded, DMA_DONE)
            act.wait_ge(b1_loaded, DMA_DONE)
            act.wait_ge(hidden_summed, 1)
            for t in range(BLOCKS):
                act.activation(hidden_sigmoid[:, t, :], hidden_sum[:, t, :], ACT.Sigmoid,
                               bias=b1_cols[:, t:t + 1]).then_inc(sigmoid_set, 1)
            act.wait_ge(gate_summed, 1)
            act.activation(gate[:, :], gate_sum[:, :], ACT.Sigmoid).then_inc(gate_set, 1)
            with act.Fori(0, ROUNDS) as rnd:
                for s in range(SLOTS):
                    act.wait_ge(chunk_scaled, rnd * SLOTS + (s + 1))
                    act.dma_start(out[:, steps(rnd, s), :], ring[:, s, :, :]).then_inc(chunk_stored[s], DMA_DONE)
            for s in range(SLOTS):
                act.wait_ge(chunk_stored[s], ROUNDS * DMA_DONE)

        @block.vector
        def _(dve):
            dve.wait_ge(cond_turned, 1)
            dve.tensor_copy(cond_t[:, :, :].rearrange("k c b -> k (c b)"), turned_cond[:, :]).then_inc(cond_t_set, 1)
            for c in range(BLOCKS):
                dve.wait_ge(w1_turned, c + 1)
                dve.tensor_copy(w1_t[:, c, :, :].rearrange("k t p -> k (t p)"), turned[c][:, :]).then_inc(w1_t_set, 1)
            dve.wait_ge(b1_loaded, DMA_DONE)
            dve.wait_ge(sigmoid_set, BLOCKS)
            for t in range(BLOCKS):
                dve.scalar_tensor_tensor(out=hidden[:, t, :], in0=hidden_sum[:, t, :], scalar=b1_cols[:, t:t + 1],
                                         in1=hidden_sigmoid[:, t, :], op0=ALU.add, op1=ALU.mult).then_inc(hidden_set, 1)
            for t in range(BLOCKS):
                dve.wait_ge(w2_turned, t + 1)
                dve.tensor_copy(w2_t[:, t, :], turned[t][:, :]).then_inc(w2_t_set, 1)
            dve.wait_ge(gate_set, 1)
            dve.tensor_scalar_add(factor[:, :], gate[:, :], 2.0).then_inc(factor_set, 1)
            dve.wait_ge(factor_set, 1)
            factor_steps = factor[:, :].unsqueeze(1).to_broadcast([P, CHUNK_STEPS, D])
            with dve.Fori(0, ROUNDS) as rnd:
                for s in range(SLOTS):
                    dve.wait_ge(chunk_loaded[s], (rnd + 1) * DMA_DONE)
                    dve.tensor_tensor(ring[:, s, :, :], ring[:, s, :, :], factor_steps,
                                      ALU.mult).then_inc(chunk_scaled, 1)


INPUTS = ["x", "cond_1024", "L0_cond_W1", "L0_cond_b1", "L0_cond_W2", "L0_cond_b2"]


def kernel(**inputs):
    import numpy as np
    import concourse.bacc as bacc
    from concourse.bass_utils import run_bass_kernel_spmd

    nc = bacc.Bacc("TRN2", target_bir_lowering=False, num_devices=1)
    arrays, args = {}, []
    for name in INPUTS:
        a = np.ascontiguousarray(inputs[name])
        arrays[f"in_{name}"] = a
        args.append(nc.dram_tensor(f"in_{name}", a.shape, mybir.dt.from_np(a.dtype), kind="ExternalInput").ap())
    out = nc.dram_tensor("out", inputs["x"].shape, F32, kind="ExternalOutput").ap()
    gated_residual_program(nc, *args, out)
    result = run_bass_kernel_spmd(nc, [arrays], core_ids=[0])
    return result.results[0]["out"]
```

```python
from contextlib import ExitStack

import concourse.bass as bass
from concourse import mybir

F32 = mybir.dt.float32
ALU = mybir.AluOpType
ACT = mybir.ActivationFunctionType

P = 128
CHUNK_STEPS = 8
GROUPS = 2
SLOTS = 8
DMA_DONE = 16


def gated_residual_program(nc, x, cond, w1, b1, w2, b2, out):
    B, N, D = x.shape
    BLOCKS = D // P
    SAMPLES = B // GROUPS
    assert B == P and D == BLOCKS * P and N == GROUPS * SLOTS * CHUNK_STEPS and GROUPS >= 2
    x_parts = x.rearrange("(g q) (h n) d -> g (q h) n d", g=GROUPS, h=GROUPS)
    out_parts = out.rearrange("(g q) (h n) d -> g (q h) n d", g=GROUPS, h=GROUPS)

    with ExitStack() as ctx:
        def sbuf(name, shape):
            return ctx.enter_context(nc.sbuf_tensor(name, shape, F32))

        def psum(name, shape):
            return ctx.enter_context(nc.psum_tensor(name, shape, F32))

        def sem(name):
            return ctx.enter_context(nc.semaphore(name))

        ring = sbuf("ring", [P, SLOTS, CHUNK_STEPS, D])
        cond_rows = sbuf("cond_rows", [P, D])
        w1_rows = sbuf("w1_rows", [P, BLOCKS, D])
        w2_rows = sbuf("w2_rows", [P, BLOCKS, D])
        b1_cols = sbuf("b1_cols", [P, BLOCKS])
        b2_row = sbuf("b2_row", [1, D])
        identity = sbuf("identity", [P, P])
        ones_row = sbuf("ones_row", [1, P])
        cond_t = sbuf("cond_t", [P, BLOCKS, B])
        w1_t = sbuf("w1_t", [P, BLOCKS, BLOCKS, P])
        w2_t = sbuf("w2_t", [P, BLOCKS, D])
        hidden_sigmoid = sbuf("hidden_sigmoid", [P, BLOCKS, B])
        hidden = sbuf("hidden", [P, BLOCKS, B, GROUPS])
        gate = sbuf("gate", [P, GROUPS, D])
        factor = sbuf("factor", [P, GROUPS, D])

        turned = [psum(f"turned{c}", [P, D]) for c in range(BLOCKS)]
        turned_cond = psum("turned_cond", [P, D])
        hidden_sum = psum("hidden_sum", [P, BLOCKS, B])
        gate_sum = [psum(f"gate_sum{g}", [P, D]) for g in range(GROUPS)]

        cond_loaded, w1_loaded, w2_loaded = sem("cond_loaded"), sem("w1_loaded"), sem("w2_loaded")
        b1_loaded, b2_loaded = sem("b1_loaded"), sem("b2_loaded")
        zeros_set, identity_set, ones_set = sem("zeros_set"), sem("identity_set"), sem("ones_set")
        cond_turned, w1_turned, w2_turned = sem("cond_turned"), sem("w1_turned"), sem("w2_turned")
        cond_t_set, w1_t_set, w2_t_set = sem("cond_t_set"), sem("w1_t_set"), sem("w2_t_set")
        hidden_summed, sigmoid_set, hidden_set = sem("hidden_summed"), sem("sigmoid_set"), sem("hidden_set")
        gate_summed, gate_set, factor_set = sem("gate_summed"), sem("gate_set"), sem("factor_set")
        chunk_loaded = [sem(f"chunk_loaded{s}") for s in range(SLOTS)]
        chunk_scaled = sem("chunk_scaled")
        chunk_stored = [sem(f"chunk_stored{s}") for s in range(SLOTS)]

        block = ctx.enter_context(nc.Block())

        def chunk(parts, g, s):
            return parts[bass.ds(g, 1), :, s * CHUNK_STEPS:(s + 1) * CHUNK_STEPS, :].rearrange("g p n d -> (g p) n d")

        @block.sync
        def _(sp):
            sp.dma_start(w1_rows[:, :, :], w1.rearrange("(p t) k -> p t k", t=BLOCKS)).then_inc(w1_loaded, DMA_DONE)
            sp.dma_start(cond_rows[:, :], cond).then_inc(cond_loaded, DMA_DONE)
            sp.dma_start(w2_rows[:, :, :], w2.rearrange("(t p) k -> p t k", p=P)).then_inc(w2_loaded, DMA_DONE)
            for s in range(SLOTS):
                sp.dma_start(ring[:, s, :, :], chunk(x_parts, 0, s)).then_inc(chunk_loaded[s], DMA_DONE)
            with sp.Fori(1, GROUPS) as g:
                for s in range(SLOTS):
                    sp.wait_ge(chunk_stored[s], g * DMA_DONE)
                    sp.dma_start(ring[:, s, :, :], chunk(x_parts, g, s)).then_inc(chunk_loaded[s], DMA_DONE)

        @block.gpsimd
        def _(pool):
            pool.memset(identity[:, :], 0.0).then_inc(zeros_set, 1)
            pool.memset(ones_row[:, :], 1.0).then_inc(ones_set, 1)
            pool.wait_ge(zeros_set, 1)
            pool.affine_select(out=identity[:, :], in_=identity[:, :], compare_op=ALU.not_equal, fill=1.0,
                               base=0, pattern=[[-1, P]], channel_multiplier=1).then_inc(identity_set, 1)

        @block.tensor
        def _(pe):
            pe.wait_ge(identity_set, 1)
            pe.wait_ge(cond_loaded, DMA_DONE)
            for c in range(BLOCKS):
                last = pe.transpose(turned_cond[:, c * B:(c + 1) * B], cond_rows[:, c * P:(c + 1) * P], identity[:, :])
            last.then_inc(cond_turned, 1)
            pe.wait_ge(w1_loaded, DMA_DONE)
            for c in range(BLOCKS):
                for t in range(BLOCKS):
                    last = pe.transpose(turned[c][:, t * P:(t + 1) * P], w1_rows[:, t, c * P:(c + 1) * P],
                                        identity[:, :])
                last.then_inc(w1_turned, 1)
            pe.wait_ge(cond_t_set, 1)
            pe.wait_ge(w1_t_set, BLOCKS)
            for t in range(BLOCKS):
                for c in range(BLOCKS):
                    last = pe.matmul(hidden_sum[:, t, :], w1_t[:, c, t, :], cond_t[:, c, :],
                                     start=(c == 0), stop=(c == BLOCKS - 1))
            last.then_inc(hidden_summed, 1)
            pe.wait_ge(w2_loaded, DMA_DONE)
            w2_strided = w2_rows[:, :, :].rearrange("j m (p t) -> j m t p", t=BLOCKS)
            for t in range(BLOCKS):
                for m in range(BLOCKS):
                    last = pe.transpose(turned[t][:, m * P:(m + 1) * P], w2_strided[:, m, t, :], identity[:, :])
                last.then_inc(w2_turned, 1)
            pe.wait_ge(ones_set, 1)
            pe.wait_ge(b2_loaded, DMA_DONE)
            pe.wait_ge(hidden_set, BLOCKS)
            pe.wait_ge(w2_t_set, BLOCKS)
            for g in range(GROUPS):
                pe.matmul(gate_sum[g][:, :], ones_row[:, :], b2_row[:, :], start=True, stop=False)
                for t in range(BLOCKS):
                    samples = hidden[:, t, g * SAMPLES:(g + 1) * SAMPLES, :].rearrange("p q h -> p (q h)")
                    last = pe.matmul(gate_sum[g][:, :], samples, w2_t[:, t, :], start=False, stop=(t == BLOCKS - 1))
                last.then_inc(gate_summed, 1)

        @block.scalar
        def _(act):
            act.dma_start(b1_cols[:, :], b1.rearrange("(p t) -> p t", t=BLOCKS)).then_inc(b1_loaded, DMA_DONE)
            act.dma_start(b2_row[:, :], b2.rearrange("(a j) -> a j", a=1)).then_inc(b2_loaded, DMA_DONE)
            act.wait_ge(b1_loaded, DMA_DONE)
            act.wait_ge(hidden_summed, 1)
            for t in range(BLOCKS):
                act.activation(hidden_sigmoid[:, t, :], hidden_sum[:, t, :], ACT.Sigmoid,
                               bias=b1_cols[:, t:t + 1]).then_inc(sigmoid_set, 1)
            for g in range(GROUPS):
                act.wait_ge(gate_summed, g + 1)
                act.activation(gate[:, g, :], gate_sum[g][:, :], ACT.Sigmoid).then_inc(gate_set, 1)
            with act.Fori(0, GROUPS) as g:
                for s in range(SLOTS):
                    act.wait_ge(chunk_scaled, g * SLOTS + (s + 1))
                    act.dma_start(chunk(out_parts, g, s), ring[:, s, :, :]).then_inc(chunk_stored[s], DMA_DONE)
            for s in range(SLOTS):
                act.wait_ge(chunk_stored[s], GROUPS * DMA_DONE)

        @block.vector
        def _(dve):
            dve.wait_ge(cond_turned, 1)
            dve.tensor_copy(cond_t[:, :, :].rearrange("k c b -> k (c b)"), turned_cond[:, :]).then_inc(cond_t_set, 1)
            for c in range(BLOCKS):
                dve.wait_ge(w1_turned, c + 1)
                dve.tensor_copy(w1_t[:, c, :, :].rearrange("k t p -> k (t p)"), turned[c][:, :]).then_inc(w1_t_set, 1)
            dve.wait_ge(b1_loaded, DMA_DONE)
            dve.wait_ge(sigmoid_set, BLOCKS)
            for t in range(BLOCKS):
                dve.scalar_tensor_tensor(out=hidden[:, t, :, :],
                                         in0=hidden_sum[:, t, :].unsqueeze(2).to_broadcast([P, B, GROUPS]),
                                         scalar=b1_cols[:, t:t + 1],
                                         in1=hidden_sigmoid[:, t, :].unsqueeze(2).to_broadcast([P, B, GROUPS]),
                                         op0=ALU.add, op1=ALU.mult).then_inc(hidden_set, 1)
            for t in range(BLOCKS):
                dve.wait_ge(w2_turned, t + 1)
                dve.tensor_copy(w2_t[:, t, :], turned[t][:, :]).then_inc(w2_t_set, 1)
            dve.wait_ge(gate_set, GROUPS)
            dve.tensor_scalar_add(factor[:, :, :], gate[:, :, :], 2.0).then_inc(factor_set, 1)
            dve.wait_ge(factor_set, 1)
            with dve.Fori(0, GROUPS) as g:
                factor_steps = factor[:, bass.ds(g, 1), :].to_broadcast([P, CHUNK_STEPS, D])
                for s in range(SLOTS):
                    dve.wait_ge(chunk_loaded[s], (g + 1) * DMA_DONE)
                    dve.tensor_tensor(ring[:, s, :, :], ring[:, s, :, :], factor_steps,
                                      ALU.mult).then_inc(chunk_scaled, 1)


INPUTS = ["x", "cond_1024", "L0_cond_W1", "L0_cond_b1", "L0_cond_W2", "L0_cond_b2"]


def kernel(**inputs):
    import numpy as np
    import concourse.bacc as bacc
    from concourse.bass_utils import run_bass_kernel_spmd

    nc = bacc.Bacc("TRN2", target_bir_lowering=False, num_devices=1)
    arrays, args = {}, []
    for name in INPUTS:
        a = np.ascontiguousarray(inputs[name])
        arrays[f"in_{name}"] = a
        args.append(nc.dram_tensor(f"in_{name}", a.shape, mybir.dt.from_np(a.dtype), kind="ExternalInput").ap())
    out = nc.dram_tensor("out", inputs["x"].shape, F32, kind="ExternalOutput").ap()
    gated_residual_program(nc, *args, out)
    result = run_bass_kernel_spmd(nc, [arrays], core_ids=[0])
    return result.results[0]["out"]
```
